# Optimizing a Trainium2 kernel written in Bass

```python
import numpy as np
import jax
import jax.numpy as jnp

def _softmax(x, axis=-1):
    return jax.nn.softmax(x, axis=axis)

def _gelu(x):
    return jax.nn.gelu(x, approximate=True)

def _silu(x):
    return jax.nn.silu(x)

def _sigmoid(x):
    return jax.nn.sigmoid(x)

def _layernorm(x, axis=-1, eps=1e-05):
    m = jnp.mean(x, axis=axis, keepdims=True)
    v = jnp.var(x, axis=axis, keepdims=True)
    return (x - m) / jnp.sqrt(v + eps)

def _scatter_add(tgt, idx, src, axis=0):
    return tgt.at[idx].add(src)

def _segment_sum(src, seg, n):
    return jax.ops.segment_sum(src, seg, n)
kernel_name = 'mk_seq_preln_d1_jaxref_r4_fa48b6'

def setup_inputs(seed: int=0):
    np.random.seed(seed)
    _w = jnp.asarray

    def _L0_attn_setup():
        import jax, jax.numpy as jnp
        import numpy as np
        H = 16
        W = 128
        NEG = -1000000000.0
        key = jax.random.key(seed)
        k1, k2 = jax.random.split(key)
        x = jax.random.normal(k1, (4, 1024, 256), dtype=jnp.float32)
        w_qkv = jax.random.normal(k2, (256, 768), dtype=jnp.float32) * 0.02
        return {'x': x, 'w_qkv': w_qkv}
    _L0_attn_in = _L0_attn_setup()

    def _L0_ffn_setup():
        import jax, jax.numpy as jnp
        import numpy as np
        ALPHA = 1.702
        LIMIT = 7.0
        K = 2
        key = jax.random.key(seed)
        ks = jax.random.split(key, 4)
        B, S, H, E, I = (1, 256, 256, 8, 256)
        return {'hidden_states': jax.random.normal(ks[0], (B, S, H), jnp.float32), 'router_weight': jax.random.normal(ks[1], (E, H), jnp.float32), 'router_bias': jnp.zeros((E,), jnp.float32), 'gate_up_proj': jax.random.normal(ks[2], (E, H, 2 * I), jnp.float32) * 0.02, 'gate_up_bias': jnp.zeros((E, 2 * I), jnp.float32), 'down_proj': jax.random.normal(ks[3], (E, I, H), jnp.float32) * 0.02, 'down_bias': jnp.zeros((E, H), jnp.float32)}
    _L0_ffn_in = _L0_ffn_setup()
    _d = {'L0_attn_x': _L0_attn_in['x'], 'L0_attn_w_qkv': _L0_attn_in['w_qkv'], 'L0_ffn_router_weight': _L0_ffn_in['router_weight'], 'L0_ffn_router_bias': _L0_ffn_in['router_bias'], 'L0_ffn_gate_up_proj': _L0_ffn_in['gate_up_proj'], 'L0_ffn_gate_up_bias': _L0_ffn_in['gate_up_bias'], 'L0_ffn_down_proj': _L0_ffn_in['down_proj'], 'L0_ffn_down_bias': _L0_ffn_in['down_bias']}
    _x0 = _d['L0_attn_x']
    _d['L0_attn_x'] = jax.random.normal(jax.random.fold_in(jax.random.key(seed), 1), (32, 512, 256), dtype=_x0.dtype)
    del _x0
    return _d

def reference(L0_attn_x, L0_attn_w_qkv, L0_ffn_router_weight, L0_ffn_router_bias, L0_ffn_gate_up_proj, L0_ffn_gate_up_bias, L0_ffn_down_proj, L0_ffn_down_bias):

    def _L0_attn_ref(x, w_qkv):
        import jax, jax.numpy as jnp
        import numpy as np
        H = 16
        W = 128
        NEG = -1000000000.0
        B, L, D = x.shape
        E = D // H
        nw = L // W
        qkv = x @ w_qkv
        q, k, v = jnp.split(qkv, 3, axis=-1)

        def to_win(t):
            return t.reshape(B, L, H, E).transpose(0, 2, 1, 3).reshape(B, H, nw, W, E)
        q, k, v = map(to_win, (q, k, v))
        pad = lambda t: jnp.pad(t, ((0, 0), (0, 0), (1, 1), (0, 0), (0, 0)))
        kp, vp = (pad(k), pad(v))
        k_ctx = jnp.concatenate([kp[:, :, i:i + nw] for i in range(3)], axis=3)
        v_ctx = jnp.concatenate([vp[:, :, i:i + nw] for i in range(3)], axis=3)
        scale = E ** (-0.5)
        scores = jnp.einsum('bhnqe,bhnke->bhnqk', q * scale, k_ctx)
        key_pos = (jnp.arange(nw)[:, None] - 1) * W + jnp.arange(3 * W)[None, :]
        valid = (key_pos >= 0) & (key_pos < L)
        scores = jnp.where(valid[None, None, :, None, :], scores, NEG)
        attn = jax.nn.softmax(scores, axis=-1)
        out = jnp.einsum('bhnqk,bhnke->bhnqe', attn, v_ctx)
        return out.reshape(B, H, L, E).transpose(0, 2, 1, 3).reshape(B, L, D)

    def _L0_ffn_ref(hidden_states, router_weight, router_bias, gate_up_proj, gate_up_bias, down_proj, down_bias):
        import jax, jax.numpy as jnp
        import numpy as np
        ALPHA = 1.702
        LIMIT = 7.0
        K = 2
        B, S, H = hidden_states.shape
        E = router_weight.shape[0]
        I = down_proj.shape[1]
        T = B * S
        flat = hidden_states.reshape(T, H)
        logits = flat @ router_weight.T + router_bias
        scores = jax.nn.softmax(logits, axis=-1)
        topk_vals, topk_idx = jax.lax.top_k(scores, K)
        w = jnp.zeros((T, E), scores.dtype).at[jnp.arange(T)[:, None], topk_idx].set(topk_vals)
        gu = jnp.einsum('th,ehf->tef', flat, gate_up_proj) + gate_up_bias
        gate = jnp.minimum(gu[..., :I], LIMIT)
        up = jnp.clip(gu[..., I:], -LIMIT, LIMIT)
        glu = gate * jax.nn.sigmoid(gate * ALPHA)
        act = (up + 1.0) * glu
        down = jnp.einsum('tei,eih->teh', act, down_proj) + down_bias
        out = jnp.einsum('teh,te->th', down, w)
        return out.reshape(B, S, H)
    x = L0_attn_x
    x = x + _L0_attn_ref(_layernorm(x, axis=-1), L0_attn_w_qkv)
    x = x + _L0_ffn_ref(_layernorm(x, axis=-1), L0_ffn_router_weight, L0_ffn_router_bias, L0_ffn_gate_up_proj, L0_ffn_gate_up_bias, L0_ffn_down_proj, L0_ffn_down_bias)
    return x

_drawn_inputs = setup_inputs


def setup_inputs(seed=0):
    import zlib

    import numpy as np

    out = dict(_drawn_inputs(seed))
    spreads = {'L0_ffn_router_bias': (0.0, 2.0),
     'L0_ffn_gate_up_bias': (0.0, 0.439),
     'L0_ffn_down_bias': (0.0, 0.1)}
    factors = {'L0_attn_w_qkv': 2.871}
    for name, (base, spread) in spreads.items():
        noise = np.random.default_rng([zlib.crc32(name.encode()), seed]).standard_normal(out[name].shape)
        drawn = base * np.exp(spread * noise) if base else spread * noise
        out[name] = jnp.asarray(drawn.astype(out[name].dtype))
    for name, factor in factors.items():
        out[name] = (out[name] * factor).astype(out[name].dtype)
    return out
```

```python
from contextlib import ExitStack

import concourse.bass as bass
from concourse import mybir

F32 = mybir.dt.float32
F22 = mybir.dt.float32r
BF16 = mybir.dt.bfloat16
U32 = mybir.dt.uint32
I32 = mybir.dt.int32
ALU = mybir.AluOpType
ACT = mybir.ActivationFunctionType
X = mybir.AxisListType.X

P = 128
EPS = 1e-5
HEADS = 16
HD = 16
HALF = HEADS // 2
GROUP = 4
NGROUP = HEADS // GROUP
HROW = 32
Q_PART = (0, 0, 1, 0, 2, 1)
K_PART = (0, 1, 0, 2, 0, 1)
STRIPS = len(Q_PART)
KROWS = STRIPS * HD
UNITS = 3
CROWS = 3
TOPK = 2
ALPHA = 1.702
LIMIT = 7.0


class Step:

    def __init__(self, turn, const, in_loop, n, unroll):
        self.turn, self.const, self.in_loop, self.n, self.unroll = turn, const, in_loop, n, unroll

    def back(self, d):
        if not self.in_loop and not 0 <= self.const - d < self.n:
            return None
        return Step(self.turn, self.const - d, self.in_loop, self.n, self.unroll)

    @property
    def par(self):
        return self.const % 2

    @property
    def index(self):
        return self.turn * self.unroll + self.const if self.in_loop else self.const

    def count(self, per, k=0):
        return self.value(self.unroll * per, self.const * per + k)

    def count_par(self, per, k=0, ring=2):
        return self.value(self.unroll // ring * per, self.const // ring * per + k)

    def value(self, per_turn, first):
        assert first > 0 or not self.in_loop
        return self.turn * per_turn + first if self.in_loop else first


def reach(engine, sem, value):
    if not isinstance(value, int) or value > 0:
        engine.wait_ge(sem, value)


def wait_apart(engine, sem, value, passed):
    engine.wait_ge(sem, value)
    engine.sem_inc(passed, 1)


def pipeline(engine, n, before, after, body, ahead=1, unroll=2):
    last = n - ahead
    for i in range(before):
        body(Step(0, i, False, n, unroll))
    assert (last - before) % unroll == 0 and unroll % 2 == 0
    with engine.Fori(0, (last - before) // unroll) as turn:
        for u in range(unroll):
            body(Step(turn, before + u, True, n, unroll))
    for i in range(last, n + after):
        body(Step(0, i, False, n, unroll))


SCHEDULE = (
    (0, "a", "c1", 2, True), (0, "b", "xt0", 0, True), (1, "a", "pv3", 3, False), (1, "b", "o3", 3, True),
    (2, "a", "xt1", 0, True), (3, "a", "qk0", 0, True), (4, "b", "stats2", 3, False), (5, "a", "qk1", 0, True),
    (5, "b", "pv0", 2, False), (5, "b", "norm2", 3, False), (6, "a", "ht0", 3, True), (6, "b", "o0", 2, True),
    (7, "a", "ht1", 3, True), (7, "a", "max0", 1, False), (7, "b", "qk2", 0, True), (8, "a", "c0", 1, True),
    (8, "b", "route", 3, True), (9, "a", "turn", 3, True), (10, "a", "pick", 3, False), (10, "a", "qk3", 0, True),
    (10, "b", "pv1", 2, False), (11, "b", "stats1", -1, False), (11, "b", "v0", 1, True), (11, "b", "o1", 2, True),
    (12, "a", "norm1", -1, False), (12, "b", "rank", 3, True), (13, "a", "place", 3, False),
    (13, "a", "pv2", 2, False), (14, "a", "o2", 2, True), (15, "b", "scatter", 3, False), (15, "b", "max1", 1, False),
    (15, "b", "v1", 1, True),
)
BANK_USES = tuple((name, lag) for _, _, name, lag, bank in SCHEDULE if bank)
SHIFTS = {"act": {}, "dve": {}, "pool": {}}
A_BEFORE, A_AFTER = 5, 3


def uses_at(i, nb):
    return [name for name, lag in BANK_USES if 0 <= i - lag < nb]


def ticket(step, name):
    if step.in_loop:
        first = sum(len(uses_at(i, step.n)) for i in range(A_BEFORE))
        order = [u[0] for u in BANK_USES]
        per = len(order)
        return step.count(per, first + order.index(name) - A_BEFORE * per)
    before = sum(len(uses_at(i, step.n)) for i in range(step.const))
    return before + uses_at(step.const, step.n).index(name)


def steps(engine, i, slot, when, does):
    shift = SHIFTS.get(engine, {})
    for at, w, name, lag, _ in SCHEDULE:
        if 2 * at + "ab".index(w) + shift.get(name, 0) == 2 * slot + "ab".index(when) and i.back(lag):
            does(name, i.back(lag))


def block_kernel(nc, x_in, w_qkv, router_w, router_b, gu_w, gu_b, dn_w, dn_b, out):
    NB, L, D = x_in.shape
    NW = L // P
    KC = D // P
    E, _, F2 = gu_w.shape
    FI = F2 // 2
    T = NB * L
    NT = T // P
    CAP = T + P
    SPARE = E * CAP
    SLOTS = TOPK * NT + E
    QK_CHUNKS = 2 * KC
    assert NW == 4 and D == 256 and HEADS * HD == D and E == 8

    x_rows = x_in.rearrange("b (n p) d -> b p n d", p=P)
    out_rows = out.rearrange("b (n p) d -> b p n d", p=P)
    parts_dram = nc.dram_tensor("qk_parts", [2, 2, 3, D, L], BF16).ap()
    x2_dram = nc.dram_tensor("x2_rows", [NB, P, NW, D], F32).ap()
    sorted_dram = nc.dram_tensor("expert_in", [SPARE + E * P, D], F32).ap()
    y_dram = nc.dram_tensor("expert_out", [SLOTS * P, D], F32).ap()

    ctx = ExitStack()
    with ctx:
        def sb(name, shape, dt=F32, where=ctx):
            return where.enter_context(nc.sbuf_tensor(name, shape, dt))

        def sem(name):
            return ctx.enter_context(nc.semaphore(name))

        ident = sb("ident", [P, P])
        ident_bf = sb("ident_bf", [P, P], BF16)
        pos_all = sb("pos_all", [P, NT * TOPK])
        ypos = sb("ypos", [P, NT * TOPK], U32)
        w_all = sb("w_all", [P, NT * TOPK])
        run = sb("run", [P, E])
        region = sb("region", [P, E + 1])
        iota_e = sb("iota_e", [P, E + 1])
        bgu = sb("bgu", [P, E, F2])
        biases_loaded = sem("biases_loaded")

        a_mem = ExitStack()
        A = lambda name, shape, dt=F32: sb(name, shape, dt, a_mem)
        wqkv = A("wqkv", [P, KC, 3 * D])
        rw = A("rw", [E, D])
        rwT = A("rwT", [P, KC, HROW])
        logitT = A("logitT", [P, P])
        rbias = A("rbias", [P, E])
        half_neg = A("half_neg", [P, NW])
        upper = A("upper", [P, P], BF16)
        ones_bf = A("ones_bf", [P, P], BF16)
        xin = A("xin", [P, NW, D])
        xn = A("xn", [P, NW, D])
        stats = A("stats", [P, 2, NW, 6])
        mv = A("mv", [P, 2, NW, 2])
        rstd = A("rstd", [P, 2, NW])
        xnT = A("xnT", [P, 2, KC, L])
        parts = A("parts", [P, 3, QK_CHUNKS, L], BF16)
        resid = A("resid", [P, 2, L])
        qs = A("qs", [P, 2, HEADS, L], BF16)
        ks = A("ks", [P, 2, HEADS, L], BF16)
        vt = A("vt", [P, 2, NW, HEADS, HROW])
        negmax = A("negmax", [P, HEADS, NW])
        cpart = A("cpart", [P, CROWS, HALF * NW], BF16)
        crest = A("crest", [P, HALF * NW])
        crow = A("crow", [CROWS * HALF * NW, 2, P], BF16)
        WA = 2 * 2 * P
        WB = 2 * 3 * P
        prob = A("prob", [P, 2, GROUP, WA + WB])
        oT = A("oT", [P, L])
        osum = A("osum", [P, NW, GROUP])
        onorm = A("onorm", [P, 2, NW, GROUP * HD])
        x2 = A("x2", [P, 2, NW, D])
        h2 = A("h2", [P, 2, NW, D])
        h2T = A("h2T", [P, KC, L])
        logit = A("logit", [P, NW, E])
        score = A("score", [P, NW, E])
        lsum = A("lsum", [P, 2, NW])
        top = A("top", [P, NW, 8])
        top_i = A("top_i", [P, NW, 8], U32)
        pick = A("pick", [P, NW, TOPK])
        onehot = A("onehot", [P, NW * TOPK, E])
        chosen = A("chosen", [P, NW, E], BF16)
        rank = A("rank", [P, NW, E])
        place = A("place", [P, NW * TOPK, E])
        posf = A("posf", [P, NW * TOPK])
        pos = A("pos", [P, 2, NW * TOPK], U32)

        ps_mem = ExitStack()
        bankA = ps_mem.enter_context(nc.psum_tensor("rowsA", [P, 512], F32))
        bankB = ps_mem.enter_context(nc.psum_tensor("rowsB", [P, 2, 512], F32))
        keysA = ps_mem.enter_context(nc.psum_tensor("keysA", [P, 512], F32))
        keysB = ps_mem.enter_context(nc.psum_tensor("keysB", [P, 2, 512], F32))
        attn = ps_mem.enter_context(nc.psum_tensor("attn", [P, 512], F32))
        bank = ps_mem.enter_context(nc.psum_tensor("shared_bank", [P, 512], F32))
        bank_bf = bank[:, :].bitcast(BF16)

        passed_dve, passed_pool, passed_sp = (sem(f"passed_{n}") for n in ("dve", "pool", "sp"))
        const_loaded = sem("const_loaded")
        const_ready = sem("const_ready")
        ones_ready = [sem(f"ones_ready{q}") for q in range(2)]
        spares_written = sem("spares_written")
        pool_seq = sem("pool_seq")
        rw_turned = sem("rw_turned")
        rw_ready = sem("rw_ready")
        x_loaded = sem("x_loaded")
        ln1_seq = sem("ln1_seq")
        ln1_rstd = sem("ln1_rstd")
        xn_ready = sem("xn_ready")
        bank_full = sem("bank_full")
        bank_free = sem("bank_free")
        hi_ready = sem("hi_ready")
        mid_ready = sem("mid_ready")
        lo_ready = sem("lo_ready")
        parts_written = [sem(f"parts_written{h}") for h in range(2)]
        stacked = [[sem(f"stacked{p}{h}") for h in range(2)] for p in range(2)]
        rows_ready = sem("rows_ready")
        max_done = sem("max_done")
        c_seq = sem("c_seq")
        c_landed = [[sem(f"c_landed{p}{h}") for h in range(2)] for p in range(2)]
        keys_ready = sem("keys_ready")
        exp_done = sem("exp_done")
        pv_done = sem("pv_done")
        oT_ready = sem("oT_ready")
        osum_ready = sem("osum_ready")
        x2_added = sem("x2_added")
        res_loaded = [sem(f"res_loaded{p}") for p in range(2)]
        x2_stored = [sem(f"x2_stored{p}") for p in range(2)]
        ln2_seq = sem("ln2_seq")
        ln2_rstd = sem("ln2_rstd")
        h2_ready = sem("h2_ready")
        route_seq = sem("route_seq")
        route_exp = sem("route_exp")
        chosen_ready = sem("chosen_ready")
        place_seq = sem("place_seq")
        pos_ready = sem("pos_ready")
        scattered = [sem(f"scattered{p}") for p in range(2)]

        with a_mem, ps_mem:
            block = a_mem.enter_context(nc.Block())

            @block.sync
            def _(sp):
                sp.dma_start(xin[:, :, :], x_rows[0]).then_inc(x_loaded, 16)
                sp.dma_start(wqkv[:, :, :], w_qkv.rearrange("(k p) n -> p k n", p=P)).then_inc(const_loaded, 16)
                sp.dma_start(rw[:, :], router_w).then_inc(const_loaded, 16)
                sp.dma_start(rbias[:, :], router_b.partition_broadcast(P)).then_inc(const_loaded, 16)
                sp.dma_start(bgu[:, :, :], gu_b.partition_broadcast(P)).then_inc(biases_loaded, 16)
                sp.dma_start(sorted_dram[SPARE:, :].rearrange("(b t) d -> b t d", t=L), x_in[0:E * P // L])\
                    .then_inc(spares_written, 16)

                def write_parts(p, half):
                    wait_apart(sp, lo_ready, p.count(4, 2 * half + 2), passed_sp)
                    reach(sp, stacked[p.par][half], p.count_par(2 * STRIPS * 16))
                    for qk in range(2):
                        sp.dma_start(parts_dram[p.par, qk, :, half * P:(half + 1) * P, :].rearrange("c r t -> r c t"),
                                     parts[:, :, 2 * half + qk, :]).then_inc(parts_written[half], 16)

                def stack(p, half):
                    if not p.in_loop and p.const < 2 and half == 0:
                        sp.wait_ge(ones_ready[p.par], 1)
                    wait_apart(sp, parts_written[half], p.count(32, 32), passed_sp)
                    reach(sp, keys_ready, p.count(2 * HEADS, -4 * HEADS + HEADS * (half + 1)))
                    for qk, (dst, which) in enumerate(((qs, Q_PART), (ks, K_PART))):
                        for s, part in enumerate(which):
                            src = parts_dram[p.par, qk, part, half * P:(half + 1) * P, :]
                            sp.dma_start(dst[s * HD:(s + 1) * HD, p.par, half * HALF:(half + 1) * HALF, :],
                                         src.rearrange("(h e) t -> e h t", e=HD)).then_inc(stacked[p.par][half], 16)

                def c_rows(b, i, half):
                    sp.wait_ge(bank_free, ticket(i, f"c{half}") + 1)
                    for c in range(CROWS):
                        n = HALF * NW
                        dst = qs[KROWS + c:KROWS + c + 1, b.par, half * HALF:(half + 1) * HALF, :]
                        sp.dma_start(dst.rearrange("o h (n t) -> o (h n) t", t=P),
                                     crow[c * n:(c + 1) * n, half, :]).then_inc(c_landed[b.par][half], 16)

                def body(i):
                    nxt, p, s, t, f = (i.back(d) for d in (-1, 0, 1, 2, 3))
                    if t:
                        if t.back(2):
                            wait_apart(sp, x2_stored[t.par], t.count_par(16), passed_sp)
                            sp.wait_ge(h2_ready, t.count(1, -1))
                        sp.dma_start(x2[:, t.par, :, :], x_rows[t.index]).then_inc(res_loaded[t.par], 16)
                        c_rows(t, i, 1)
                    if nxt:
                        sp.wait_ge(xn_ready, nxt.count(1))
                        sp.dma_start(xin[:, :, :], x_rows[nxt.index]).then_inc(x_loaded, 16)
                    if f:
                        sp.wait_ge(x2_added, f.count(NGROUP, NGROUP))
                        sp.dma_start(x2_dram[f.index], x2[:, f.par, :, :]).then_inc(x2_stored[f.par], 16)
                    if p:
                        write_parts(p, 0)
                        stack(p, 0)
                    if s:
                        c_rows(s, i, 0)
                    if p:
                        write_parts(p, 1)
                        stack(p, 1)

                pipeline(sp, NB, A_BEFORE, A_AFTER, body)
                for q in range(2):
                    sp.wait_ge(x2_stored[q], 16 * (NB // 2))
                sp.wait_ge(spares_written, 16)

            @block.gpsimd
            def _(pool):
                done = [0]

                def link(ins):
                    done[0] += 1
                    ins.then_inc(pool_seq, 1)
                    pool.wait_ge(pool_seq, done[0])

                def iota(dst, pattern, channel=0):
                    link(pool.iota(dst, pattern, base=0, channel_multiplier=channel,
                                   allow_small_or_imprecise_dtypes=True))

                link(pool.memset(ident[:, :], 0.0))
                link(pool.memset(upper[:, :], 1.0))
                link(pool.memset(ones_bf[:, :], 1.0))
                link(pool.memset(half_neg[:, :], -0.5))
                iota(iota_e[:, :], [[1, E + 1]])
                iota(run[:, :], [[CAP, E]])
                iota(region[:, :], [[CAP, E + 1]])
                link(pool.affine_select(out=ident[:, :], in_=ident[:, :], compare_op=ALU.not_equal, fill=1.0, base=0,
                                        pattern=[[-1, P]], channel_multiplier=1))
                link(pool.affine_select(out=upper[:, :], in_=upper[:, :], compare_op=ALU.is_gt, fill=0.0, base=0,
                                        pattern=[[1, P]], channel_multiplier=-1))
                link(pool.tensor_copy(ident_bf[:, :], ident[:, :]))
                link(pool.memset(rwT[:, :, :], 0.0))
                link(pool.memset(vt[:, :, :, :, :], 0.0))
                pool.memset(vt[:, :, :, :, HD:HD + 1], 1.0).then_inc(const_ready, 1)
                pool.wait_ge(const_ready, 1)

                def rstd_of(which, seq, done, b):
                    wait_apart(pool, seq, b.count(2, 2), passed_pool)
                    pool.tensor_scalar(rstd[:, which, :], mv[:, which, :, 1], EPS, None, ALU.add).then_inc(done, 1)
                    pool.wait_ge(done, b.count(2, 1))
                    pool.tensor_tensor(rstd[:, which, :], rstd[:, which, :], half_neg[:, :], ALU.pow).then_inc(done, 1)

                def split(p, i, c):
                    reach(pool, parts_written[c // 2], p.count(32))
                    wait_apart(pool, bank_free, ticket(i, f"qk{c}") + 1, passed_pool)
                    r = resid[:, c % 2, :]
                    pool.tensor_copy(parts[:, 1, c, :], r).then_inc(mid_ready, 1)
                    pool.wait_ge(mid_ready, p.count(4, c + 1))
                    pool.tensor_tensor(parts[:, 2, c, :], r, parts[:, 1, c, :], ALU.subtract).then_inc(lo_ready, 1)

                def add_heads(b, i, g):
                    pool.wait_ge(bank_free, ticket(i, f"o{g}") + 1)
                    pool.wait_ge(res_loaded[b.par], b.count_par(16, 16))
                    cols = x2[:, b.par, :, g * GROUP * HD:(g + 1) * GROUP * HD]
                    pool.tensor_tensor(cols, cols, onorm[:, g % 2, :, :], ALU.add).then_inc(x2_added, 1)

                def scatter(f):
                    wait_apart(pool, pos_ready, f.count(1, 1), passed_pool)
                    for c in range(NW * TOPK):
                        pool.indirect_dma_start(
                            sorted_dram, bass.IndirectOffsetOnAxis(pos[:, f.par, c:c + 1], 0),
                            h2[:, f.par, c // TOPK, :], None).then_inc(scattered[f.par], 16)

                first = Step(0, 0, False, NB, 2)
                rstd_of(0, ln1_seq, ln1_rstd, first)
                pool.wait_ge(ln1_rstd, 2)
                pool.memset(ks[KROWS:KROWS + HROW, 1, :, :], 1.0).then_inc(ones_ready[1], 1)
                pool.wait_ge(ones_ready[1], 1)

                def body(i):
                    def does(name, b):
                        if name == "stats1":
                            rstd_of(0, ln1_seq, ln1_rstd, b)
                        elif name == "stats2":
                            rstd_of(1, ln2_seq, ln2_rstd, b)
                        elif name[:2] == "qk":
                            split(b, i, int(name[2]))
                        elif name in ("o0", "o1", "o2", "o3"):
                            add_heads(b, i, int(name[1]))
                        elif name == "scatter":
                            scatter(b)

                    for slot in range(HEADS):
                        steps("pool", i, slot, "a", does)
                        steps("pool", i, slot, "b", does)

                pipeline(pool, NB, A_BEFORE, A_AFTER, body)
                for q in range(2):
                    pool.wait_ge(scattered[q], 16 * NW * TOPK * (NB // 2))

            @block.scalar
            def _(act):
                act.wait_ge(const_ready, 1)
                act.wait_ge(rw_turned, 1)
                act.copy(rwT[:, :, 0:E], bank[:, 0:KC * E].rearrange("p (k e) -> p k e", k=KC)).then_inc(rw_ready, 1)

                def exps(t, h):
                    g, q = h // GROUP, h % GROUP
                    dst = prob[:, g % 2, q, :]
                    if q == 0:
                        reach(act, pv_done, t.count(NGROUP, g - 1))
                    act.wait_ge(keys_ready, t.count(2 * HEADS, 2 * h + 1))
                    act.activation(dst[:, 0:WA], keysA[:, :], ACT.Exp, scale=HD ** -0.5).then_inc(exp_done, 1)
                    act.wait_ge(keys_ready, t.count(2 * HEADS, 2 * h + 2))
                    act.activation(dst[:, WA:].rearrange("p (w c) -> p w c", w=2), keysB[:, :, 0:3 * P], ACT.Exp,
                                   scale=HD ** -0.5).then_inc(exp_done, 1)

                def take_attn(b, g):
                    act.wait_ge(pv_done, b.count(NGROUP, g + 1))
                    reach(act, osum_ready, b.count(NGROUP, g))
                    act.copy(oT[:, :], attn[:, :]).then_inc(oT_ready, 1)

                def body(i):
                    def take(name, dst, src):
                        act.wait_ge(bank_full, ticket(i, name) + 1)
                        act.copy(dst, src).then_inc(bank_free, 1)

                    def does(name, b):
                        if name in ("c0", "c1"):
                            half = int(name[1])
                            if b.back(1):
                                act.wait_ge(c_landed[1 - b.par][half], b.back(1).count_par(16 * CROWS, 16 * CROWS))
                            take(name, crow[:, half, :], bank_bf[0:CROWS * HALF * NW, 0:P])
                        elif name[:2] == "xt":
                            take(name, xnT[:, b.par, int(name[2]), :], bank[:, :])
                        elif name[:2] == "ht":
                            take(name, h2T[:, int(name[2]), :], bank[:, :])
                        elif name in ("v0", "v1"):
                            w = 2 * int(name[1])
                            take(name, vt[:, b.par, w:w + 2, :, 0:HD],
                                 bank[:, :].rearrange("p (n h e) -> p n h e", n=2, h=HEADS))
                        elif name == "route":
                            take(name, logitT[:, :], bank[:, 0:P])
                        elif name[:2] == "qk":
                            c = int(name[2])
                            reach(act, parts_written[c // 2], b.count(32))
                            act.wait_ge(bank_full, ticket(i, name) + 1)
                            act.copy(parts[:, 0, c, :], bank[:, :]).then_inc(hi_ready, 1)
                        elif name[:2] == "pv":
                            take_attn(b, int(name[2]))
                        elif name == "pick":
                            act.wait_ge(route_seq, b.count(8, 2))
                            act.activation(score[:, :, :], logit[:, :, :], ACT.Exp).then_inc(route_exp, 1)

                    t = i.back(2)
                    for slot in range(HEADS):
                        steps("act", i, slot, "a", does)
                        if t:
                            exps(t, slot)
                        steps("act", i, slot, "b", does)

                pipeline(act, NB, A_BEFORE, A_AFTER, body)

            @block.vector
            def _(dve):
                def norm(which, seq, b, src):
                    for n in range(NW):
                        last = dve.bn_stats(stats[:, which, n, :], src(n))
                    last.then_inc(seq, 1)
                    wait_apart(dve, seq, b.count(2, 1), passed_dve)
                    for n in range(NW):
                        last = dve.bn_aggr(mv[:, which, n, :], stats[:, which, n, :])
                    last.then_inc(seq, 1)

                def apply(which, rs, ready, b, src, dst):
                    dve.wait_ge(rs, b.count(2, 2))
                    for n in range(NW):
                        last = dve.tensor_scalar(dst(n), src(n), mv[:, which, n, 0:1], rstd[:, which, n:n + 1],
                                                 ALU.subtract, ALU.mult)
                    last.then_inc(ready, 1)

                def ln1_stats(b):
                    dve.wait_ge(x_loaded, b.count(16, 16))
                    norm(0, ln1_seq, b, lambda n: xin[:, n, :])

                def ln1_apply(b, i):
                    if i is not None:
                        dve.wait_ge(bank_full, ticket(i, "xt1") + 1)
                    dve.wait_ge(ln1_seq, b.count(2, 2))
                    apply(0, ln1_rstd, xn_ready, b, lambda n: xin[:, n, :], lambda n: xn[:, n, :])

                dve.wait_ge(const_loaded, 48)
                dve.wait_ge(const_ready, 1)
                first = Step(0, 0, False, NB, 2)
                ln1_stats(first)
                ln1_apply(first, None)
                dve.memset(ks[KROWS:KROWS + HROW, 0, :, :], 1.0).then_inc(ones_ready[0], 1)

                def row_max(s, h):
                    dve.wait_ge(rows_ready, s.count(UNITS * HEADS, UNITS * h + 1))
                    dve.tensor_reduce(negmax[:, h, 0:NW:NW - 1], bankA[:, :].rearrange("p (w c) -> p w c", w=2), X,
                                      ALU.max, negate=True).then_inc(max_done, 1)
                    for u in range(2):
                        dve.wait_ge(rows_ready, s.count(UNITS * HEADS, UNITS * h + 2 + u))
                        dve.tensor_reduce(negmax[:, h, 1 + u:2 + u], bankB[:, u, 0:3 * P], X, ALU.max,
                                          negate=True).then_inc(max_done, 1)

                def c_parts(s, i, half):
                    before = (i, "c1") if half == 0 else (i, "c0")
                    src = negmax[:, half * HALF:(half + 1) * HALF, :].rearrange("p h n -> p (h n)")
                    dve.wait_ge(max_done, s.count(UNITS * HEADS, UNITS * HALF * (half + 1)))
                    if half == 1 or s.back(1):
                        dve.wait_ge(bank_full, ticket(*before) + 1)
                    dve.tensor_copy(cpart[:, 0, :], src).then_inc(c_seq, 1)
                    dve.wait_ge(c_seq, s.count(8, 4 * half + 1))
                    dve.tensor_tensor(crest[:, :], src, cpart[:, 0, :], ALU.subtract).then_inc(c_seq, 1)
                    dve.wait_ge(c_seq, s.count(8, 4 * half + 2))
                    dve.tensor_copy(cpart[:, 1, :], crest[:, :]).then_inc(c_seq, 1)
                    dve.wait_ge(c_seq, s.count(8, 4 * half + 3))
                    dve.tensor_tensor(cpart[:, 2, :], crest[:, :], cpart[:, 1, :], ALU.subtract).then_inc(c_seq, 1)

                def divide(b, i, g):
                    dve.wait_ge(bank_full, ticket(i, f"o{g}") + 1)
                    o = bank[:, :].rearrange("p (n h c) -> p n h c", n=NW, h=GROUP)
                    dve.reciprocal(osum[:, :, :], o[:, :, :, HD]).then_inc(osum_ready, 1)
                    dve.wait_ge(osum_ready, b.count(NGROUP, g + 1))
                    reach(dve, x2_added, b.count(NGROUP, g - 1))
                    dve.tensor_tensor(onorm[:, g % 2, :, :].rearrange("p n (h c) -> p n h c", h=GROUP), o[:, :, :, 0:HD],
                                      osum[:, :, :].unsqueeze(3).broadcast_to([P, NW, GROUP, HD]),
                                      ALU.mult).then_inc(bank_free, 1)

                def route_logits(f, i):
                    dve.wait_ge(bank_full, ticket(i, "turn") + 1)
                    dve.tensor_tensor(logit[:, :, :], bank[:, 0:P].rearrange("p (n e) -> p n e", n=NW)[:, :, 0:E],
                                      rbias[:, :].unsqueeze(1).broadcast_to([P, NW, E]), ALU.add).then_inc(bank_free, 1)
                    dve.wait_ge(bank_free, ticket(i, "turn") + 1)
                    dve.tensor_reduce(lsum[:, 0, :], logit[:, :, :], X, ALU.max, negate=True).then_inc(route_seq, 1)
                    dve.wait_ge(route_seq, f.count(8, 1))
                    dve.tensor_tensor(logit[:, :, :], logit[:, :, :],
                                      lsum[:, 0, :].unsqueeze(2).broadcast_to([P, NW, E]), ALU.add).then_inc(route_seq, 1)

                def route_pick(f):
                    dve.wait_ge(route_exp, f.count(1, 1))
                    dve.tensor_reduce(lsum[:, 1, :], score[:, :, :], X, ALU.add).then_inc(route_seq, 1)
                    dve.wait_ge(route_seq, f.count(8, 3))
                    dve.reciprocal(lsum[:, 1, :], lsum[:, 1, :]).then_inc(route_seq, 1)
                    dve.wait_ge(route_seq, f.count(8, 4))
                    dve.tensor_tensor(score[:, :, :], score[:, :, :],
                                      lsum[:, 1, :].unsqueeze(2).broadcast_to([P, NW, E]), ALU.mult).then_inc(route_seq, 1)
                    wait_apart(dve, route_seq, f.count(8, 5), passed_dve)
                    for n in range(NW):
                        last = dve.max(top[:, n, :], score[:, n, :])
                    last.then_inc(route_seq, 1)
                    wait_apart(dve, route_seq, f.count(8, 6), passed_dve)
                    for n in range(NW):
                        last = dve.max_index(top_i[:, n, :], top[:, n, :], score[:, n, :])
                    last.then_inc(route_seq, 1)
                    dve.tensor_copy(w_all[:, bass.ds(f.count(NW * TOPK), NW * TOPK)].rearrange("p (n s) -> p n s", s=TOPK),
                                    top[:, :, 0:TOPK])
                    dve.wait_ge(route_seq, f.count(8, 7))
                    dve.tensor_copy(pick[:, :, :], top_i[:, :, 0:TOPK]).then_inc(route_seq, 1)
                    dve.wait_ge(route_seq, f.count(8, 8))
                    dve.tensor_tensor(onehot[:, :, :], iota_e[:, 0:E].unsqueeze(1).broadcast_to([P, NW * TOPK, E]),
                                      pick[:, :, :].rearrange("p n s -> p (n s)").unsqueeze(2)
                                      .broadcast_to([P, NW * TOPK, E]), ALU.is_equal).then_inc(chosen_ready, 1)
                    dve.wait_ge(chosen_ready, f.count(2, 1))
                    oh = onehot[:, :, :].rearrange("p (n s) e -> p n s e", s=TOPK)
                    dve.tensor_tensor(chosen[:, :, :], oh[:, :, 0, :], oh[:, :, 1, :], ALU.add).then_inc(chosen_ready, 1)

                def route_rank(f, i):
                    dve.wait_ge(bank_full, ticket(i, "rank") + 1)
                    dve.tensor_tensor(rank[:, :, :], bank[:, 0:NW * E].rearrange("p (n e) -> p n e", n=NW),
                                      run[:, :].unsqueeze(1).broadcast_to([P, NW, E]), ALU.add).then_inc(place_seq, 1)
                    dve.wait_ge(place_seq, f.count(3, 1))
                    dve.tensor_tensor(run[:, :], run[:, :], bank[:, NW * E:(NW + 1) * E], ALU.add).then_inc(bank_free, 1)

                def route_place(f):
                    dve.tensor_tensor(place[:, :, :].rearrange("p (n s) e -> p n s e", s=TOPK),
                                      onehot[:, :, :].rearrange("p (n s) e -> p n s e", s=TOPK),
                                      rank[:, :, :].unsqueeze(2).broadcast_to([P, NW, TOPK, E]),
                                      ALU.mult).then_inc(place_seq, 1)
                    dve.wait_ge(place_seq, f.count(3, 2))
                    dve.tensor_reduce(posf[:, :], place[:, :, :], X, ALU.add).then_inc(place_seq, 1)
                    dve.wait_ge(place_seq, f.count(3, 3))
                    reach(dve, scattered[f.par], f.count_par(16 * NW * TOPK))
                    dve.tensor_copy(pos_all[:, bass.ds(f.count(NW * TOPK), NW * TOPK)], posf[:, :])
                    dve.tensor_copy(pos[:, f.par, :], posf[:, :]).then_inc(pos_ready, 1)

                def body(i):
                    def does(name, b):
                        if name in ("o0", "o1", "o2", "o3"):
                            divide(b, i, int(name[1]))
                        elif name == "stats1":
                            ln1_stats(b)
                        elif name == "norm1":
                            ln1_apply(b, i)
                        elif name == "stats2":
                            dve.wait_ge(x2_added, b.count(NGROUP, NGROUP))
                            norm(1, ln2_seq, b, lambda n: x2[:, b.par, n, :])
                        elif name == "norm2":
                            reach(dve, scattered[b.par], b.count_par(16 * NW * TOPK))
                            apply(1, ln2_rstd, h2_ready, b, lambda n: x2[:, b.par, n, :], lambda n: h2[:, b.par, n, :])
                        elif name[:2] == "qk":
                            c = int(name[2])
                            reach(dve, lo_ready, b.count(4, c - 1))
                            dve.wait_ge(hi_ready, b.count(4, c + 1))
                            dve.tensor_tensor(resid[:, c % 2, :], bank[:, :], parts[:, 0, c, :],
                                              ALU.subtract).then_inc(bank_free, 1)
                        elif name in ("max0", "max1"):
                            c_parts(b, i, int(name[3]))
                        elif name == "turn":
                            route_logits(b, i)
                        elif name == "pick":
                            route_pick(b)
                        elif name == "place":
                            route_place(b)
                        elif name == "rank":
                            route_rank(b, i)

                    s = i.back(1)
                    for slot in range(HEADS):
                        if s:
                            row_max(s, slot)
                        steps("dve", i, slot, "a", does)
                        steps("dve", i, slot, "b", does)

                pipeline(dve, NB, A_BEFORE, A_AFTER, body)

            @block.tensor
            def _(pe):
                pe.wait_ge(const_loaded, 48)
                pe.wait_ge(const_ready, 1)
                for k in range(KC):
                    last = pe.transpose(bank[:, k * E:(k + 1) * E], rw[:, k * P:(k + 1) * P], ident[0:E, 0:E])
                last.then_inc(rw_turned, 1)
                pe.wait_ge(rw_ready, 1)

                def row_scores(s, h):
                    if h % HALF == 0:
                        half = h // HALF
                        pe.wait_ge(stacked[s.par][half], s.count_par(2 * STRIPS * 16, 2 * STRIPS * 16))
                    q, k = qs[0:KROWS, s.par, h, :], ks[0:KROWS, s.par, h, :]
                    reach(pe, max_done, s.count(UNITS * HEADS, UNITS * (h - 1) + 1))
                    pe.matmul(bankA[:, 0:2 * P], q[:, 0:P], k[:, 0:2 * P], start=True, stop=True)
                    pe.matmul(bankA[:, 2 * P:], q[:, 3 * P:], k[:, 2 * P:], start=True, stop=True).then_inc(rows_ready, 1)
                    for u in range(2):
                        reach(pe, max_done, s.count(UNITS * HEADS, UNITS * (h - 1) + 2 + u))
                        pe.matmul(bankB[:, u, 0:3 * P], q[:, (1 + u) * P:(2 + u) * P], k[:, u * P:(u + 3) * P],
                                  start=True, stop=True).then_inc(rows_ready, 1)

                def key_scores(t, h):
                    if h % HALF == 0:
                        pe.wait_ge(c_landed[t.par][h // HALF], t.count_par(16 * CROWS, 16 * CROWS))
                    q, k = qs[0:KROWS + CROWS, t.par, h, :], ks[0:KROWS + CROWS, t.par, h, :]
                    reach(pe, exp_done, t.count(2 * HEADS, 2 * h - 1))
                    pe.matmul(keysA[:, 0:2 * P], k[:, 0:P], q[:, 0:2 * P], start=True, stop=True)
                    pe.matmul(keysA[:, 2 * P:], k[:, 3 * P:], q[:, 2 * P:], start=True, stop=True).then_inc(keys_ready, 1)
                    reach(pe, exp_done, t.count(2 * HEADS, 2 * h))
                    pe.matmul(keysB[:, 0, 0:3 * P], k[:, P:2 * P], q[:, 0:3 * P], start=True, stop=True)
                    pe.matmul(keysB[:, 1, 0:3 * P], k[:, 2 * P:3 * P], q[:, P:], start=True, stop=True)\
                        .then_inc(keys_ready, 1)

                def weigh_values(b, g):
                    pe.wait_ge(exp_done, b.count(2 * HEADS, 2 * GROUP * (g + 1)))
                    reach(pe, oT_ready, b.count(NGROUP, g))
                    plan = ((0, 0, 2 * P, 0), (1, WA, 3 * P, 0), (2, WA + 3 * P, 3 * P, P), (3, 2 * P, 2 * P, 2 * P))
                    for w, c0, n, q0 in plan:
                        for q in range(GROUP):
                            h = g * GROUP + q
                            last = pe.matmul(attn[q * HROW:(q + 1) * HROW, q0:q0 + n], vt[:, b.par, w, h, :],
                                             prob[:, g % 2, q, c0:c0 + n], start=(w == 0), stop=(w == NW - 1),
                                             tile_position=(0, q * HROW), skip_group_check=True)
                    last.then_inc(pv_done, 1)

                def turn_rows(src, ident_):
                    for n in range(NW):
                        last = pe.transpose(bank[:, n * P:(n + 1) * P], src(n), ident_)
                    return last

                def body(i):
                    def does(name, b):
                        if name[:2] == "pv":
                            weigh_values(b, int(name[2]))
                            return
                        if name not in [u[0] for u in BANK_USES]:
                            return
                        reach(pe, bank_free, ticket(i, name))
                        if name[:2] == "xt":
                            k = int(name[2])
                            pe.wait_ge(xn_ready, b.count(1, 1))
                            last = turn_rows(lambda n: xn[:, n, k * P:(k + 1) * P], ident[:, :])
                        elif name[:2] == "qk":
                            c = int(name[2])
                            col = (c % 2) * D + (c // 2) * P
                            for k in range(KC):
                                last = pe.matmul(bank[:, :], wqkv[:, k, col:col + P], xnT[:, b.par, k, :],
                                                 start=(k == 0), stop=(k == KC - 1))
                        elif name in ("v0", "v1"):
                            for n in range(2):
                                w = 2 * int(name[1]) + n
                                for k in range(KC):
                                    last = pe.matmul(bank[:, n * D:(n + 1) * D], xnT[:, b.par, k, w * P:(w + 1) * P],
                                                     wqkv[:, k, 2 * D:], start=(k == 0), stop=(k == KC - 1))
                        elif name in ("c0", "c1"):
                            pe.wait_ge(c_seq, b.count(8, 4 * int(name[1]) + 4))
                            last = pe.transpose(bank_bf[0:CROWS * HALF * NW, 0:P],
                                                cpart[:, :, :].rearrange("p c r -> p (c r)"), ident_bf[:, :])
                        elif name in ("o0", "o1", "o2", "o3"):
                            pe.wait_ge(oT_ready, b.count(NGROUP, int(name[1]) + 1))
                            last = turn_rows(lambda n: oT[:, n * P:(n + 1) * P], ident[:, :])
                        elif name[:2] == "ht":
                            k = int(name[2])
                            pe.wait_ge(h2_ready, b.count(1, 1))
                            last = turn_rows(lambda n: h2[:, b.par, n, k * P:(k + 1) * P], ident[:, :])
                        elif name == "route":
                            for k in range(KC):
                                for n in range(NW):
                                    last = pe.matmul(bank[n * HROW:(n + 1) * HROW, 0:P], rwT[:, k, :],
                                                     h2T[:, k, n * P:(n + 1) * P], start=(k == 0), stop=(k == KC - 1),
                                                     tile_position=(0, n * HROW), skip_group_check=True)
                        elif name == "turn":
                            last = pe.transpose(bank[:, 0:P], logitT[:, :], ident[:, :])
                        elif name == "rank":
                            pe.wait_ge(chosen_ready, b.count(2, 2))
                            for n in range(NW + 1):
                                for m in range(min(n + 1, NW)):
                                    last = pe.matmul(bank[:, n * E:(n + 1) * E],
                                                     (upper if m == n else ones_bf)[:, :], chosen[:, m, :],
                                                     start=(m == 0), stop=(m == min(n, NW - 1)))
                        last.then_inc(bank_full, 1)

                    s, t = i.back(1), i.back(2)
                    for slot in range(HEADS):
                        if s:
                            row_scores(s, slot)
                        steps("pe", i, slot, "a", does)
                        if t:
                            key_scores(t, slot)
                        steps("pe", i, slot, "b", does)

                pipeline(pe, NB, A_BEFORE, A_AFTER, body)

        RING = 4
        b_mem = ExitStack()
        M = lambda name, shape, dt=F32: sb(name, shape, dt, b_mem)
        wst = M("wst", [P, RING, KC * F2 + FI // P * D])
        w_hi = M("w_hi", [P, E, KC * F2 + FI // P * D], F22)
        w_lo = M("w_lo", [P, E, KC * F2 + FI // P * D], F22)
        tile_expert = M("tile_expert", [P, SLOTS], I32)
        tile_row = M("tile_row", [P, SLOTS], I32)
        bdn = M("bdn", [P, E, D])
        zeros = M("zeros", [P, D])
        iota_p = M("iota_p", [P, 1])
        iota_j = M("iota_j", [P, NT])
        iota_s = M("iota_s", [P, SLOTS])
        padf = M("padf", [P, E])
        pad = M("pad", [P, E], U32)
        cnt = M("cnt", [P, E])
        over = M("over", [P, E, NT])
        tiles = M("tiles", [P, E])
        start = M("start", [P, E + 1])
        shift = M("shift", [P, E + 1])
        cmp = M("cmp", [P, SLOTS, E + 1])
        eid = M("eid", [P, SLOTS])
        rowf = M("rowf", [P, SLOTS])
        xt = M("xt", [P, RING, D])
        step = M("step", [P, E - 1])
        back = M("back", [P, NT * TOPK])
        hT = M("hT", [P, 2, D])
        hT_hi = M("hT_hi", [P, 2, D], F22)
        hT_lo = M("hT_lo", [P, 2, D], F22)
        pre = M("pre", [P, 2, F2])
        gate = M("gate", [P, 2, FI])
        up = M("up", [P, 2, FI])
        th = M("th", [P, 2, FI])
        glu = M("glu", [P, 2, FI])
        hid = M("hid", [P, 2, FI])
        hidT = M("hidT", [P, 2, FI])
        hidT_hi = M("hidT_hi", [P, 2, FI], F22)
        hidT_lo = M("hidT_lo", [P, 2, FI], F22)
        yt = M("yt", [P, RING, D])
        pb_mem = ExitStack()
        psX = pb_mem.enter_context(nc.psum_tensor("psX", [P, 2, 512], F32))
        psG = pb_mem.enter_context(nc.psum_tensor("psG", [P, 2, 512], F32))
        psA = pb_mem.enter_context(nc.psum_tensor("psA", [P, 2, 512], F32))
        psD = pb_mem.enter_context(nc.psum_tensor("psD", [P, 2, 512], F32))
        weights_loaded = [sem(f"weights_loaded{q}") for q in range(RING)]
        whi_ready = sem("whi_ready")
        wlo_ready = sem("wlo_ready")
        iotas_ready = sem("iotas_ready")
        pads_ready = sem("pads_ready")
        padded = sem("padded")
        table_seq = sem("table_seq")
        table_ready = sem("table_ready")
        xt_loaded = [sem(f"xt_loaded{q}") for q in range(RING)]
        xT_done = sem("xT_done")
        hT_ready = sem("hT_ready")
        hTlo_ready = sem("hTlo_ready")
        gu_done = sem("gu_done")
        pre_ready = sem("pre_ready")
        gate_ready = sem("gate_ready")
        tanh_done = sem("tanh_done")
        glu_ready = sem("glu_ready")
        hid_ready = sem("hid_ready")
        turned = sem("turned")
        hidT_ready = sem("hidT_ready")
        hidTlo_ready = sem("hidTlo_ready")
        dn_done = sem("dn_done")
        y_ready = sem("y_ready")
        y_stored = [sem(f"y_stored{q}") for q in range(RING)]
        GU, HID, TURN, DN, BIAS, ST = 1, 2, 3, 4, 5, 9
        B_BEFORE, B_AFTER = 12, ST

        with b_mem, pb_mem:
            block = b_mem.enter_context(nc.Block())

            def slots(engine, body):
                pipeline(engine, SLOTS, B_BEFORE, B_AFTER, body, ahead=0, unroll=RING)

            def load_expert(engine, ring, b):
                engine.reg_load(ring[b.const % RING], tile_expert[0:1, bass.ds(b.count(1), 1)])

            def expert_of(engine, ring, b):
                return engine.snap(ring[b.const % RING], min_val=0, max_val=E - 1)

            @block.sync
            def _(sp):
                gate_up = gu_w.rearrange("e (k p) f -> e p k f", p=P)
                down = dn_w.rearrange("e (k p) f -> e p k f", p=P)
                for e in range(E):
                    q = e % RING
                    if e >= RING:
                        sp.wait_ge(wlo_ready, e - RING + 1)
                    sp.dma_start(wst[:, q, 0:KC * F2].rearrange("p (k f) -> p k f", k=KC), gate_up[e])\
                        .then_inc(weights_loaded[q], 16)
                    sp.dma_start(wst[:, q, KC * F2:].rearrange("p (k f) -> p k f", k=FI // P), down[e])\
                        .then_inc(weights_loaded[q], 16)
                sp.dma_start(bdn[:, :, :], dn_b.partition_broadcast(P)).then_inc(biases_loaded, 16)
                sp.wait_ge(table_ready, 1)
                sp.wait_ge(padded, 16 * E)

                def row_of(b):
                    return sp.value_load(tile_row[0:1, bass.ds(b.count(1), 1)], min_val=0,
                                         max_val=SPARE + (E - 1) * P)

                def body(i):
                    b, d = i.back(0), i.back(ST)
                    if b:
                        reach(sp, xT_done, b.count(1, 1 - RING))
                        q = b.const % RING
                        sp.dma_start(xt[:, q, :], sorted_dram[bass.ds(row_of(b), P), :]).then_inc(xt_loaded[q], 16)
                    if d:
                        sp.wait_ge(y_ready, d.count(1, 1))
                        q = d.const % RING
                        sp.dma_start(y_dram[bass.ds(d.count(P), P), :], yt[:, q, :]).then_inc(y_stored[q], 16)

                slots(sp, body)
                for q in range(RING):
                    sp.wait_ge(y_stored[q], 16 * (SLOTS // RING))

            @block.gpsimd
            def _(pool):
                for n, (dst, step, size, channel) in enumerate(((iota_p, 0, 1, 1), (iota_j, P, NT, 0),
                                                                 (iota_s, 1, SLOTS, 0))):
                    pool.iota(dst[:, :], [[step, size]], base=0, channel_multiplier=channel,
                              allow_small_or_imprecise_dtypes=True).then_inc(iotas_ready, 1)
                    pool.wait_ge(iotas_ready, n + 1)
                pool.memset(zeros[:, :], 0.0).then_inc(iotas_ready, 1)
                pool.wait_ge(iotas_ready, 4)
                pool.wait_ge(pads_ready, 1)
                for e in range(E):
                    pool.indirect_dma_start(sorted_dram, bass.IndirectOffsetOnAxis(pad[:, e:e + 1], 0),
                                            zeros[:, :], None).then_inc(padded, 16)

                def body(i):
                    x, a = i.back(0), i.back(TURN)
                    if x:
                        pool.wait_ge(hT_ready, x.count(1, 1))
                        reach(pool, gu_done, x.count(1, -1))
                        pool.tensor_tensor(hT_lo[:, x.par, :], hT[:, x.par, :], hT_hi[:, x.par, :],
                                           ALU.subtract).then_inc(hTlo_ready, 1)
                    if a:
                        pool.wait_ge(hidT_ready, a.count(1, 1))
                        reach(pool, dn_done, a.count(1, -1))
                        pool.tensor_tensor(hidT_lo[:, a.par, :], hidT[:, a.par, :], hidT_hi[:, a.par, :],
                                           ALU.subtract).then_inc(hidTlo_ready, 1)

                slots(pool, body)

            @block.vector
            def _(dve):
                links = [0]

                def link(ins):
                    links[0] += 1
                    ins.then_inc(table_seq, 1)
                    dve.wait_ge(table_seq, links[0])

                dve.wait_ge(iotas_ready, 4)
                link(dve.tensor_scalar(padf[:, :], run[:, :], iota_p[:, 0:1], None, ALU.add))
                dve.tensor_copy(pad[:, :], padf[:, :]).then_inc(pads_ready, 1)
                link(dve.tensor_tensor(cnt[:, :], run[:, :], region[:, 0:E], ALU.subtract))
                link(dve.tensor_tensor(over[:, :, :], cnt[:, :].unsqueeze(2).broadcast_to([P, E, NT]),
                                       iota_j[:, :].unsqueeze(1).broadcast_to([P, E, NT]), ALU.is_gt))
                link(dve.tensor_reduce(tiles[:, :], over[:, :, :], X, ALU.add))
                link(dve.memset(start[:, 0:1], 0.0))
                for e in range(E):
                    link(dve.tensor_tensor(start[:, e + 1:e + 2], start[:, e:e + 1], tiles[:, e:e + 1], ALU.add))
                link(dve.tensor_tensor(cmp[:, :, 0:E], iota_s[:, :].unsqueeze(2).broadcast_to([P, SLOTS, E]),
                                       start[:, 1:].unsqueeze(1).broadcast_to([P, SLOTS, E]), ALU.is_ge))
                link(dve.tensor_reduce(eid[:, :], cmp[:, :, 0:E], X, ALU.add))
                link(dve.scalar_tensor_tensor(shift[:, :], start[:, :], -float(P), region[:, :], ALU.mult, ALU.add))
                link(dve.tensor_tensor(cmp[:, :, :], eid[:, :].unsqueeze(2).broadcast_to([P, SLOTS, E + 1]),
                                       iota_e[:, :].unsqueeze(1).broadcast_to([P, SLOTS, E + 1]), ALU.is_equal))
                link(dve.tensor_tensor(cmp[:, :, :], cmp[:, :, :],
                                       shift[:, :].unsqueeze(1).broadcast_to([P, SLOTS, E + 1]), ALU.mult))
                link(dve.tensor_reduce(rowf[:, :], cmp[:, :, :], X, ALU.add))
                link(dve.scalar_tensor_tensor(rowf[:, :], iota_s[:, :], float(P), rowf[:, :], ALU.mult, ALU.add))
                dve.tensor_copy(tile_row[:, :], rowf[:, :])
                link(dve.tensor_scalar(eid[:, :], eid[:, :], float(E - 1), None, ALU.min))
                dve.tensor_copy(tile_expert[:, :], eid[:, :]).then_inc(table_ready, 1)
                dve.wait_ge(table_ready, 1)
                for e in range(E):
                    dve.wait_ge(whi_ready, e + 1)
                    dve.tensor_tensor(w_lo[:, e, :], wst[:, e % RING, :], w_hi[:, e, :], ALU.subtract)\
                        .then_inc(wlo_ready, 1)
                dve.wait_ge(biases_loaded, 32)
                experts = [dve.alloc_register(f"dve_expert{u}") for u in range(RING)]

                def body(i):
                    g, a, d = i.back(GU), i.back(HID), i.back(BIAS)
                    if d:
                        e = expert_of(dve, experts, d)
                        dve.wait_ge(dn_done, d.count(1, 1))
                        q = d.const % RING
                        reach(dve, y_stored[q], d.count_par(16, 0, RING))
                        dve.tensor_tensor(yt[:, q, :], psD[:, d.par, 0:D],
                                          bdn[:, bass.ds(e, 1), :].rearrange("p o f -> p (o f)"), ALU.add)\
                            .then_inc(y_ready, 1)
                    if g:
                        load_expert(dve, experts, g)
                        e = expert_of(dve, experts, g)
                    if a:
                        dve.wait_ge(tanh_done, a.count(1, 1))
                        dve.scalar_tensor_tensor(glu[:, a.par, :], th[:, a.par, :], 1.0, gate[:, a.par, :],
                                                 ALU.add, ALU.mult).then_inc(glu_ready, 1)
                    if g:
                        dve.wait_ge(gu_done, g.count(1, 1))
                        dve.tensor_tensor(pre[:, g.par, :], psG[:, g.par, :],
                                          bgu[:, bass.ds(e, 1), :].rearrange("p o f -> p (o f)"), ALU.add)\
                            .then_inc(pre_ready, 1)
                    if a:
                        dve.wait_ge(glu_ready, a.count(1, 1))
                        reach(dve, turned, a.count(1, -1))
                        dve.scalar_tensor_tensor(hid[:, a.par, :], up[:, a.par, :], 1.0, glu[:, a.par, :],
                                                 ALU.add, ALU.mult).then_inc(hid_ready, 1)
                    if g:
                        dve.wait_ge(pre_ready, g.count(1, 1))
                        dve.tensor_scalar(gate[:, g.par, :], pre[:, g.par, 0:FI], LIMIT, None, ALU.min)\
                            .then_inc(gate_ready, 1)
                        dve.tensor_scalar(up[:, g.par, :], pre[:, g.par, FI:], LIMIT, -LIMIT, ALU.min, ALU.max)

                slots(dve, body)

                link(dve.tensor_tensor(step[:, :], shift[:, 1:E], shift[:, 0:E - 1], ALU.subtract))
                wide = [P, NT * TOPK, E - 1]
                beyond = cmp[:, 0:NT * TOPK, 0:E - 1]
                link(dve.tensor_tensor(beyond, pos_all[:, :].unsqueeze(2).broadcast_to(wide),
                                       region[:, 1:E].unsqueeze(1).broadcast_to(wide), ALU.is_ge))
                link(dve.tensor_tensor(beyond, beyond,
                                       step[:, :].unsqueeze(1).broadcast_to(wide), ALU.mult))
                link(dve.tensor_reduce(back[:, :], beyond, X, ALU.add))
                link(dve.tensor_scalar(pos_all[:, :], pos_all[:, :], shift[:, 0:1], None, ALU.subtract))
                link(dve.tensor_tensor(ypos[:, :], pos_all[:, :], back[:, :], ALU.subtract))

            @block.scalar
            def _(act):
                for e in range(E):
                    act.wait_ge(weights_loaded[e % RING], 32 * (e // RING + 1))
                    act.copy(w_hi[:, e, :], wst[:, e % RING, :]).then_inc(whi_ready, 1)

                def body(i):
                    x, g, a = i.back(0), i.back(GU), i.back(TURN)
                    if x:
                        act.wait_ge(xT_done, x.count(1, 1))
                        reach(act, hTlo_ready, x.count(1, -1))
                        act.copy(hT[:, x.par, :], psX[:, x.par, 0:D])
                        reach(act, gu_done, x.count(1, -1))
                        act.copy(hT_hi[:, x.par, :], psX[:, x.par, 0:D]).then_inc(hT_ready, 1)
                    if a:
                        act.wait_ge(turned, a.count(1, 1))
                        reach(act, hidTlo_ready, a.count(1, -1))
                        act.mul(hidT[:, a.par, :], psA[:, a.par, 0:FI], 0.5)
                        reach(act, dn_done, a.count(1, -1))
                        act.mul(hidT_hi[:, a.par, :], psA[:, a.par, 0:FI], 0.5).then_inc(hidT_ready, 1)
                    if g:
                        act.wait_ge(gate_ready, g.count(1, 1))
                        reach(act, glu_ready, g.count(1, -1))
                        act.activation(th[:, g.par, :], gate[:, g.par, :], ACT.Tanh, scale=ALPHA / 2)\
                            .then_inc(tanh_done, 1)

                slots(act, body)

            @block.tensor
            def _(pe):
                pe.wait_ge(table_ready, 1)
                pe.wait_ge(wlo_ready, E)
                experts = [pe.alloc_register(f"pe_expert{u}") for u in range(RING)]

                def product(dst, hi, lo, e, first, width):
                    for k in range(KC):
                        cols = slice(first + k * width, first + (k + 1) * width)
                        rhs = [w[:, bass.ds(e, 1), cols].rearrange("p o f -> p (o f)") for w in (w_hi, w_lo)]
                        part = slice(k * P, (k + 1) * P)
                        for n, (lhs, w) in enumerate(((hi, rhs[0]), (hi, rhs[1]), (lo, rhs[0]))):
                            last = pe.matmul(dst, lhs[:, part], w, start=(k + n == 0),
                                             stop=(k == KC - 1 and n == 2))
                    return last

                def body(i):
                    x, g, a, d = i.back(0), i.back(GU), i.back(TURN), i.back(DN)
                    if x:
                        q = x.const % RING
                        pe.wait_ge(xt_loaded[q], x.count_par(16, 16, RING))
                        reach(pe, hT_ready, x.count(1, -1))
                        for k in range(KC):
                            last = pe.transpose(psX[:, x.par, k * P:(k + 1) * P], xt[:, q, k * P:(k + 1) * P],
                                                ident[:, :])
                        last.then_inc(xT_done, 1)
                    if g:
                        e = expert_of(pe, experts, g)
                        pe.wait_ge(hTlo_ready, g.count(1, 1))
                        reach(pe, pre_ready, g.count(1, -1))
                        last = product(psG[:, g.par, :], hT_hi[:, g.par, :], hT_lo[:, g.par, :], e, 0, F2)
                        last.then_inc(gu_done, 1)
                    if d:
                        e = expert_of(pe, experts, d)
                    if x:
                        load_expert(pe, experts, x)
                    if a:
                        pe.wait_ge(hid_ready, a.count(1, 1))
                        reach(pe, hidT_ready, a.count(1, -1))
                        for k in range(FI // P):
                            last = pe.transpose(psA[:, a.par, k * P:(k + 1) * P], hid[:, a.par, k * P:(k + 1) * P],
                                                ident[:, :])
                        last.then_inc(turned, 1)
                    if d:
                        pe.wait_ge(hidTlo_ready, d.count(1, 1))
                        reach(pe, y_ready, d.count(1, -1))
                        last = product(psD[:, d.par, 0:D], hidT_hi[:, d.par, :], hidT_lo[:, d.par, :], e, KC * F2, D)
                        last.then_inc(dn_done, 1)

                slots(pe, body)

        c_mem = ExitStack()
        C = lambda name, shape, dt=F32: sb(name, shape, dt, c_mem)
        res = C("res", [P, 2, NW, D])
        yg = C("yg", [P, 2, NW * TOPK, D])
        posc = C("posc", [P, 2, NW * TOPK], U32)
        wc = C("wc", [P, 2, NW * TOPK])
        posc_ready = sem("posc_ready")
        gathered = [sem(f"gathered{q}") for q in range(2)]
        resc_loaded = [sem(f"resc_loaded{q}") for q in range(2)]
        wc_ready = sem("wc_ready")
        mixed = sem("mixed")
        stored = [sem(f"stored{q}") for q in range(2)]
        with c_mem:
            block = c_mem.enter_context(nc.Block())

            def batches(engine, body):
                pipeline(engine, NB, 3, 0, body)

            @block.gpsimd
            def _(pool):
                def body(b):
                    if b.back(2):
                        wait_apart(pool, mixed, b.count(2, -2), passed_pool)
                    wait_apart(pool, posc_ready, b.count(1, 1), passed_pool)
                    for c in range(NW * TOPK):
                        pool.indirect_dma_start(yg[:, b.par, c, :], None, y_dram,
                                                bass.IndirectOffsetOnAxis(posc[:, b.par, c:c + 1], 0))\
                            .then_inc(gathered[b.par], 16)
                batches(pool, body)

            @block.sync
            def _(sp):
                def body(b):
                    reach(sp, stored[b.par], b.count_par(16))
                    sp.dma_start(res[:, b.par, :, :], x2_dram[b.index]).then_inc(resc_loaded[b.par], 16)
                batches(sp, body)

            @block.scalar
            def _(act):
                def body(b):
                    act.wait_ge(mixed, b.count(2, 2))
                    act.dma_start(out_rows[b.index], res[:, b.par, :, :]).then_inc(stored[b.par], 16)
                batches(act, body)
                for q in range(2):
                    act.wait_ge(stored[q], 16 * (NB // 2))

            @block.vector
            def _(dve):
                def row_numbers(b):
                    dve.tensor_copy(posc[:, b.par, :], ypos[:, bass.ds(b.count(NW * TOPK), NW * TOPK)])\
                        .then_inc(posc_ready, 1)

                def body(b):
                    if b.back(-1):
                        row_numbers(b.back(-1))
                    dve.tensor_copy(wc[:, b.par, :], w_all[:, bass.ds(b.count(NW * TOPK), NW * TOPK)])\
                        .then_inc(wc_ready, 1)
                    dve.wait_ge(wc_ready, b.count(1, 1))
                    dve.wait_ge(resc_loaded[b.par], b.count_par(16, 16))
                    dve.wait_ge(gathered[b.par], b.count_par(16 * NW * TOPK, 16 * NW * TOPK))
                    for s in range(TOPK):
                        if s:
                            dve.wait_ge(mixed, b.count(2, s))
                        for n in range(NW):
                            c = n * TOPK + s
                            last = dve.scalar_tensor_tensor(res[:, b.par, n, :], yg[:, b.par, c, :],
                                                            wc[:, b.par, c:c + 1], res[:, b.par, n, :],
                                                            ALU.mult, ALU.add)
                        last.then_inc(mixed, 1)
                row_numbers(Step(0, 0, False, NB, 2))
                batches(dve, body)


_INS = ["L0_attn_x", "L0_attn_w_qkv", "L0_ffn_router_weight", "L0_ffn_router_bias", "L0_ffn_gate_up_proj",
        "L0_ffn_gate_up_bias", "L0_ffn_down_proj", "L0_ffn_down_bias"]


def kernel(**inputs):
    import numpy as _np
    import concourse.bacc as _bacc
    from concourse import mybir as _mybir
    from concourse.bass_utils import run_bass_kernel_spmd as _run

    nc = _bacc.Bacc("TRN2", target_bir_lowering=False, num_devices=1)
    arrays, args = {}, []
    for name in _INS:
        a = _np.ascontiguousarray(inputs[name])
        arrays[f"in_{name}"] = a
        args.append(nc.dram_tensor(f"in_{name}", a.shape, _mybir.dt.from_np(a.dtype), kind="ExternalInput").ap())
    shape = tuple(inputs["L0_attn_x"].shape)
    args.append(nc.dram_tensor("out_x", shape, _mybir.dt.from_np(_np.dtype("float32")), kind="ExternalOutput").ap())
    block_kernel(nc, *args)
    r = _run(nc, [arrays], core_ids=[0])
    return r.results[0]["out_x"]
```
